# Optimizing a Trainium2 kernel written in Bass

```python
import numpy as np
import jax
import jax.numpy as jnp

def _softmax(x, axis=-1):
    return jax.nn.softmax(x, axis=axis)

def _gelu(x):
    return jax.nn.gelu(x, approximate=True)

def _silu(x):
    return jax.nn.silu(x)

def _sigmoid(x):
    return jax.nn.sigmoid(x)

def _layernorm(x, axis=-1, eps=1e-05):
    m = jnp.mean(x, axis=axis, keepdims=True)
    v = jnp.var(x, axis=axis, keepdims=True)
    return (x - m) / jnp.sqrt(v + eps)

def _scatter_add(tgt, idx, src, axis=0):
    return tgt.at[idx].add(src)

def _segment_sum(src, seg, n):
    return jax.ops.segment_sum(src, seg, n)
kernel_name = 'mk_adaln_ffn_d2_seqx_r8_b0f2a8'

def setup_inputs(seed: int=0):
    np.random.seed(seed)
    _w = jnp.asarray

    def _rec_inputs():
        import jax
        import jax.numpy as jnp
        _rk = jax.random.key(seed)
        x = -7.109e-05 + 0.9999 * jax.random.normal(jax.random.fold_in(_rk, 1), (128, 32, 512), jnp.float32)
        _lenS = 32 - jax.random.randint(jax.random.fold_in(_rk, 7), (128,), 0, max(1, 32 // 4) + 1, jnp.int32)
        _lenS2 = 32 - jax.random.randint(jax.random.fold_in(_rk, 8), (128,), 0, max(1, 32 // 4) + 1, jnp.int32)
        itok_B_0_15 = jax.random.randint(jax.random.fold_in(_rk, 11), (128,), 0, 16, jnp.int32)
        itok_B_0_30 = jax.random.randint(jax.random.fold_in(_rk, 12), (128,), 0, 31, jnp.int32)
        return (x, itok_B_0_15, itok_B_0_30)
    x, itok_B_0_15, itok_B_0_30 = _rec_inputs()

    def _L0_cond_setup():
        import jax, jax.numpy as jnp
        import numpy as np
        B, C, T = (64, 32, 512)
        S, D = (16, 32)
        key = jax.random.key(seed)
        k1, k2, k3 = jax.random.split(key, 3)
        x = jax.random.normal(k1, (B, C, T), dtype=jnp.float32)
        condition = jax.random.randint(k2, (B,), 0, S, dtype=jnp.int64)
        bound = float(np.sqrt(6.0 / C))
        weights = jax.random.uniform(k3, (S, C, D), dtype=jnp.float32, minval=-bound, maxval=bound)
        return {'x': x, 'condition': condition, 'weights': weights}
    _L0_cond_all = _L0_cond_setup()
    _L0_cond_in = {k: v for k, v in _L0_cond_all.items() if k in ('weights',)}
    del _L0_cond_all

    def _L0_ffn_setup():
        import math
        import jax, jax.numpy as jnp
        import numpy as np
        SCALING = 16.0 / 32.0

        def real_fourier_orthogonal_multiply(c):
            n = c.shape[-1]
            sqrt_n = math.sqrt(n)
            pair_scale = math.sqrt(n / 2.0)
            max_f = (n - 1) // 2
            work = c.astype(jnp.float32)
            dc = (work[..., 0] * sqrt_n)[..., None].astype(jnp.complex64)
            cos = work[..., 1:1 + 2 * max_f:2] * pair_scale
            sin = work[..., 2:2 + 2 * max_f:2] * pair_scale
            mid = (cos - 1j * sin).astype(jnp.complex64)
            parts = [dc, mid]
            if n % 2 == 0:
                parts.append((work[..., -1] * sqrt_n)[..., None].astype(jnp.complex64))
            spectrum = jnp.concatenate(parts, axis=-1)
            return jnp.fft.irfft(spectrum, n=n, axis=-1).astype(c.dtype)
        key = jax.random.key(seed)
        ks = jax.random.split(key, 9)
        B, S, D_in, D_out, R0, R1, E = (4, 256, 512, 512, 32, 8, 3)
        x = jax.random.normal(ks[0], (B, S, D_in), dtype=jnp.float32)
        W_base = jax.random.normal(ks[1], (D_out, D_in), dtype=jnp.float32) * 0.02
        b_base = jax.random.normal(ks[2], (D_out,), dtype=jnp.float32) * 0.02
        enc0 = jax.random.normal(ks[3], (R0, D_in), dtype=jnp.float32) * 0.02
        enc1 = jax.random.normal(ks[4], (R1, D_in), dtype=jnp.float32) * 0.02
        coefs0 = jax.random.normal(ks[5], (E, D_out, R0), dtype=jnp.float32) * 0.02
        coefs1 = jax.random.normal(ks[6], (E, D_out, R1), dtype=jnp.float32) * 0.02
        mask0 = jax.random.randint(ks[7], (E, D_out, R0), 0, 2).astype(bool)
        mask1 = jax.random.randint(ks[8], (E, D_out, R1), 0, 2).astype(bool)
        return dict(x=x, W_base=W_base, b_base=b_base, enc0=enc0, enc1=enc1, coefs0=coefs0, coefs1=coefs1, mask0=mask0, mask1=mask1)
    _L0_ffn_all = _L0_ffn_setup()
    _L0_ffn_in = {k: v for k, v in _L0_ffn_all.items() if k in ('W_base', 'b_base', 'enc0', 'enc1', 'coefs0', 'coefs1', 'mask0', 'mask1')}
    del _L0_ffn_all

    def _L1_cond_setup():
        import jax, jax.numpy as jnp
        import numpy as np
        B, C, D, T, S = (64, 32, 32, 512, 32)
        key = jax.random.key(seed)
        k1, k2, k3 = jax.random.split(key, 3)
        x = jax.random.normal(k1, (B, C, T), dtype=jnp.float32)
        subjects = jax.random.randint(k2, (B,), 0, S, dtype=jnp.int64)
        weights = jax.random.normal(k3, (S, C, D), dtype=jnp.float32) * (1.0 / np.sqrt(C))
        return {'x': x, 'subjects': subjects, 'weights': weights}
    _L1_cond_all = _L1_cond_setup()
    _L1_cond_in = {k: v for k, v in _L1_cond_all.items() if k in ('weights',)}
    del _L1_cond_all

    def _L1_ffn_setup():
        import jax, jax.numpy as jnp
        import numpy as np
        import math
        IN_DIM = 512
        FEATURES = 512
        BATCH, SEQ = (8, 256)
        key = jax.random.key(seed)
        kx, kk = jax.random.split(key)
        x = jax.random.normal(kx, (BATCH, SEQ, IN_DIM), dtype=jnp.float32)
        kernel = jax.random.randint(kk, (IN_DIM, FEATURES), 0, 2) > 0
        scale = jnp.asarray(1.0 / math.sqrt(IN_DIM), dtype=jnp.float32)
        return {'x': x, 'kernel': kernel, 'scale': scale}
    _L1_ffn_all = _L1_ffn_setup()
    _L1_ffn_in = {k: v for k, v in _L1_ffn_all.items() if k in ('kernel', 'scale')}
    del _L1_ffn_all
    return {'x': x, 'itok_B_0_15': itok_B_0_15, 'itok_B_0_30': itok_B_0_30, 'L0_cond_weights': _L0_cond_in['weights'], 'L0_ffn_W_base': _L0_ffn_in['W_base'], 'L0_ffn_b_base': _L0_ffn_in['b_base'], 'L0_ffn_enc0': _L0_ffn_in['enc0'], 'L0_ffn_enc1': _L0_ffn_in['enc1'], 'L0_ffn_coefs0': _L0_ffn_in['coefs0'], 'L0_ffn_coefs1': _L0_ffn_in['coefs1'], 'L0_ffn_mask0': _L0_ffn_in['mask0'], 'L0_ffn_mask1': _L0_ffn_in['mask1'], 'L1_cond_weights': _L1_cond_in['weights'], 'L1_ffn_kernel': _L1_ffn_in['kernel'], 'L1_ffn_scale': _L1_ffn_in['scale']}

def reference(x, itok_B_0_15, itok_B_0_30, L0_cond_weights, L0_ffn_W_base, L0_ffn_b_base, L0_ffn_enc0, L0_ffn_enc1, L0_ffn_coefs0, L0_ffn_coefs1, L0_ffn_mask0, L0_ffn_mask1, L1_cond_weights, L1_ffn_kernel, L1_ffn_scale):
    import jax
    import jax.numpy as jnp

    def _L0_cond_ref(x, condition, weights):
        import jax, jax.numpy as jnp
        import numpy as np
        B, C, T = (64, 32, 512)
        S, D = (16, 32)
        W = weights[condition]
        return jnp.einsum('bct,bcd->bdt', x, W)

    def _L0_ffn_ref(x, W_base, b_base, enc0, enc1, coefs0, coefs1, mask0, mask1):
        import math
        import jax, jax.numpy as jnp
        import numpy as np
        SCALING = 16.0 / 32.0

        def real_fourier_orthogonal_multiply(c):
            n = c.shape[-1]
            sqrt_n = math.sqrt(n)
            pair_scale = math.sqrt(n / 2.0)
            max_f = (n - 1) // 2
            work = c.astype(jnp.float32)
            dc = (work[..., 0] * sqrt_n)[..., None].astype(jnp.complex64)
            cos = work[..., 1:1 + 2 * max_f:2] * pair_scale
            sin = work[..., 2:2 + 2 * max_f:2] * pair_scale
            mid = (cos - 1j * sin).astype(jnp.complex64)
            parts = [dc, mid]
            if n % 2 == 0:
                parts.append((work[..., -1] * sqrt_n)[..., None].astype(jnp.complex64))
            spectrum = jnp.concatenate(parts, axis=-1)
            return jnp.fft.irfft(spectrum, n=n, axis=-1).astype(c.dtype)
        base = jnp.einsum('bsd,od->bso', x, W_base) + b_base
        e0 = jnp.einsum('bsd,rd->bsr', x, enc0)
        e1 = jnp.einsum('bsd,rd->bsr', x, enc1)
        w0 = coefs0 * mask0.astype(coefs0.dtype)
        w1 = coefs1 * mask1.astype(coefs1.dtype)
        decoded = jnp.einsum('bsr,eor->ebso', e0, w0) + jnp.einsum('bsr,eor->ebso', e1, w1)
        transformed = real_fourier_orthogonal_multiply(decoded)
        update = transformed.sum(axis=0)
        return base + update * SCALING

    def _L1_cond_ref(x, subjects, weights):
        import jax, jax.numpy as jnp
        import numpy as np
        B, C, D, T, S = (64, 32, 32, 512, 32)
        w = weights[subjects]
        return jnp.einsum('bct,bcd->bdt', x, w)

    def _L1_ffn_ref(x, kernel, scale):
        import jax, jax.numpy as jnp
        import numpy as np
        import math
        IN_DIM = 512
        FEATURES = 512
        BATCH, SEQ = (8, 256)
        w = kernel.astype(x.dtype) * 2.0 - 1.0
        return scale * jnp.einsum('bsi,if->bsf', x, w)
    x = x + _L0_ffn_ref(_L0_cond_ref(x, itok_B_0_15, L0_cond_weights), L0_ffn_W_base, L0_ffn_b_base, L0_ffn_enc0, L0_ffn_enc1, L0_ffn_coefs0, L0_ffn_coefs1, L0_ffn_mask0, L0_ffn_mask1)
    x = x + _L1_ffn_ref(_L1_cond_ref(x, itok_B_0_30, L1_cond_weights), L1_ffn_kernel, L1_ffn_scale)
    return x

_drawn_inputs = setup_inputs


def setup_inputs(seed=0):
    import zlib

    import numpy as np

    out = dict(_drawn_inputs(seed))
    spreads = {}
    factors = {'L0_ffn_b_base': 3.453, 'L0_ffn_enc1': 3.061, 'L0_ffn_coefs1': 3.163}
    for name, (base, spread) in spreads.items():
        noise = np.random.default_rng([zlib.crc32(name.encode()), seed]).standard_normal(out[name].shape)
        drawn = base * np.exp(spread * noise) if base else spread * noise
        out[name] = jnp.asarray(drawn.astype(out[name].dtype))
    for name, factor in factors.items():
        out[name] = (out[name] * factor).astype(out[name].dtype)
    return out
```

```python
from contextlib import ExitStack

import numpy as np
import concourse.bass as bass
from concourse import mybir
from concourse.bass import IndirectOffsetOnAxis

P = 128
SAMPLES, C, T = 128, 32, 512
PER_TILE = P // C
TILES = SAMPLES // PER_TILE
CHUNKS = T // P
KINDS0, KINDS1 = 16, 32
EXPERTS, R0, R1 = 3, 32, 8
R = R0 + R1
SCALING = 16.0 / 32.0
RING = 3
MIDDLE = TILES - 2


def fourier_basis():
    t = np.arange(T, dtype=np.float64)
    f = np.empty((T, T), np.float64)
    f[0] = 1.0 / np.sqrt(T)
    for k in range(1, (T - 1) // 2 + 1):
        angle = 2.0 * np.pi * ((k * t) % T) / T
        f[2 * k - 1] = np.sqrt(2.0 / T) * np.cos(angle)
        f[2 * k] = np.sqrt(2.0 / T) * np.sin(angle)
    f[T - 1] = np.where(t % 2 == 0, 1.0, -1.0) / np.sqrt(T)
    return f.astype(np.float32)


def build(nc, x, kind0, kind1, mix0, w_base, b_base, enc0, enc1, coefs0, coefs1, mask0, mask1,
          mix1, sign_bits, scale, basis, out):
    f32, f32r, u8 = mybir.dt.float32, mybir.dt.float32r, mybir.dt.uint8
    i32, u32 = mybir.dt.int32, mybir.dt.uint32
    ALU, ACT = mybir.AluOpType, mybir.ActivationFunctionType

    x_tiles = x.rearrange("(n s) c t -> n (s c) t", s=PER_TILE)
    out_tiles = out.rearrange("(n s) c t -> n (s c) t", s=PER_TILE)
    gathered0 = nc.dram_tensor("gathered0", (SAMPLES, C * C), f32, kind="Internal").ap()
    gathered1 = nc.dram_tensor("gathered1", (SAMPLES, C * C), f32, kind="Internal").ap()

    ctx = ExitStack()
    with ctx:
        def sb(name, shape, dt):
            return ctx.enter_context(nc.sbuf_tensor(name, shape, dt))

        def bank(name):
            return ctx.enter_context(nc.psum_tensor(name, [P, T], f32))

        def sem(name):
            return ctx.enter_context(nc.semaphore(name))

        kinds = sb("kinds", [SAMPLES, 2], i32)
        rows0 = sb("rows0", [SAMPLES, C * C], f32)
        rows1 = sb("rows1", [SAMPLES, C * C], f32)
        blocks0 = sb("blocks0", [P, TILES * P], f32)
        blocks1 = sb("blocks1", [P, TILES * P], f32)
        w_sb = sb("w_sb", [P, CHUNKS, T], f32)
        basis_sb = sb("basis_sb", [P, CHUNKS, T], f32)
        c0_sb = sb("c0_sb", [P, EXPERTS, CHUNKS * R0], f32)
        c1_sb = sb("c1_sb", [P, EXPERTS, CHUNKS * R1], f32)
        m0_sb = sb("m0_sb", [P, EXPERTS, CHUNKS * R0], u8)
        m1_sb = sb("m1_sb", [P, EXPERTS, CHUNKS * R1], u8)
        masked0 = sb("masked0", [P, EXPERTS, CHUNKS * R0], f32)
        masked1 = sb("masked1", [P, EXPERTS, CHUNKS * R1], f32)
        pair0 = sb("pair0", [P, CHUNKS * R0], f32)
        pair1 = sb("pair1", [P, CHUNKS * R1], f32)
        decode = sb("decode", [P, CHUNKS, R], f32)
        enc_sb = sb("enc_sb", [R, T], f32)
        spectrum = sb("spectrum", [R, T], f32)
        bits_sb = sb("bits_sb", [P, CHUNKS, T], u8)
        a_high = sb("a_high", [P, CHUNKS, T], f32r)
        a_low = sb("a_low", [P, CHUNKS, T], f32r)
        b_sign = sb("b_sign", [P, CHUNKS, T], f32r)
        ident = sb("ident", [P, P], f32)
        bias = sb("bias", [P, T], f32)
        scale_sb = sb("scale_sb", [P, 1], f32)

        x_in = sb("x_in", [P, RING, T], f32)
        x1 = sb("x1", [P, RING, T], f32)
        y0_high = sb("y0_high", [P, T], f32r)
        y0_low = sb("y0_low", [P, T], f32r)
        y1_high = sb("y1_high", [P, T], f32r)
        y1_low = sb("y1_low", [P, T], f32r)

        y0_ps, y1_ps, f0_ps, f1_ps = bank("y0_ps"), bank("y1_ps"), bank("f0_ps"), bank("f1_ps")
        a_ps = [bank(f"a_ps{k}") for k in range(CHUNKS)]
        spectrum_ps = f1_ps[0:R, :]

        kinds_loaded, rows0_gathered, rows1_gathered = sem("kinds_loaded"), sem("rows0_gathered"), sem("rows1_gathered")
        rows0_stored, rows1_stored = sem("rows0_stored"), sem("rows1_stored")
        blocks0_zero, blocks1_zero = sem("blocks0_zero"), sem("blocks1_zero")
        blocks0_loaded, blocks1_loaded = sem("blocks0_loaded"), sem("blocks1_loaded")
        w_loaded, basis_loaded, coefs_loaded = sem("w_loaded"), sem("basis_loaded"), sem("coefs_loaded")
        enc_loaded, bits_loaded, bias_loaded, scale_loaded = (
            sem("enc_loaded"), sem("bits_loaded"), sem("bias_loaded"), sem("scale_loaded"))
        ident_zero, ident_ready = sem("ident_zero"), sem("ident_ready")
        masked_ready, pairs_ready, decode_ready = sem("masked_ready"), sem("pairs_ready"), sem("decode_ready")
        spectrum_done, spectrum_ready = sem("spectrum_done"), sem("spectrum_ready")
        a_done, a_high_ready, a_low_ready, b_ready = sem("a_done"), sem("a_high_ready"), sem("a_low_ready"), sem("b_ready")
        x_loaded = [sem(f"x_loaded{s}") for s in range(RING)]
        stored = [sem(f"stored{s}") for s in range(RING)]
        biased = sem("biased")
        mixed0, y0_high_ready, y0_low_ready, fed0, x1_ready = (
            sem("mixed0"), sem("y0_high_ready"), sem("y0_low_ready"), sem("fed0"), sem("x1_ready"))
        mixed1, y1_high_ready, y1_low_ready, fed1, out_ready = (
            sem("mixed1"), sem("y1_high_ready"), sem("y1_low_ready"), sem("fed1"), sem("out_ready"))

        block = ctx.enter_context(nc.Block())

        @block.sync
        def _(sp):
            sp.dma_start(w_sb[:, :, :], w_base.rearrange("(c p) d -> p c d", p=P)).then_inc(w_loaded, 16)
            sp.dma_start(basis_sb[:, :, :], basis.rearrange("(p q) t -> p q t", q=CHUNKS)).then_inc(basis_loaded, 16)
            sp.dma_start(x_in[:, 0, :], x_tiles[0]).then_inc(x_loaded[0], 16)
            sp.dma_start(enc_sb[0:R0, :], enc0).then_inc(enc_loaded, 16)
            sp.dma_start(enc_sb[R0:R, :], enc1).then_inc(enc_loaded, 16)
            sp.dma_start(bias[:, :], b_base.partition_broadcast(P)).then_inc(bias_loaded, 16)
            sp.dma_start(bits_sb[:, :, :], sign_bits.rearrange("(c p) f -> p c f", p=P)).then_inc(bits_loaded, 16)
            sp.dma_start(scale_sb[:, :], scale.partition_broadcast(P)).then_inc(scale_loaded, 16)
            for slot in range(1, RING):
                sp.dma_start(x_in[:, slot, :], x_tiles[slot]).then_inc(x_loaded[slot], 16)

            def load(tile, slot):
                sp.wait_ge(mixed0, tile - RING + 1)
                sp.wait_ge(biased, tile - RING + 1)
                sp.dma_start(x_in[:, slot, :], x_tiles[bass.ds(tile, 1)].rearrange("a p t -> (a p) t")
                             ).then_inc(x_loaded[slot], 16)

            def store(tile, slot):
                sp.wait_ge(out_ready, tile + 1)
                sp.dma_start(out_tiles[bass.ds(tile, 1)].rearrange("a p t -> (a p) t"), x1[:, slot, :]
                             ).then_inc(stored[slot], 16)

            looped = (TILES - RING) // RING * RING
            with sp.Fori(0, looped, RING) as base:
                for u in range(RING):
                    load(base + u + RING, u)
                    store(base + u, u)
            for tile in range(looped, TILES):
                if tile + RING < TILES:
                    load(tile + RING, tile % RING)
                store(tile, tile % RING)
            for slot in range(RING):
                sp.wait_ge(stored[slot], 16 * len(range(slot, TILES, RING)))

        @block.gpsimd
        def _(pool):
            nc.gpsimd.memset(ident[:, :], 0.0).then_inc(ident_zero, 1)
            pool.wait_ge(ident_zero, 1)
            nc.gpsimd.affine_select(out=ident[:, :], in_=ident[:, :], compare_op=ALU.not_equal, fill=1.0, base=0,
                                    pattern=[[-1, P]], channel_multiplier=1).then_inc(ident_ready, 1)
            pool.wait_ge(kinds_loaded, 32)
            nc.gpsimd.indirect_dma_start(
                rows0[:, :], None, mix0.rearrange("k c d -> k (c d)"),
                IndirectOffsetOnAxis(kinds[:, 0:1].bitcast(u32), 0)).then_inc(rows0_gathered, 16)
            nc.gpsimd.indirect_dma_start(
                rows1[:, :], None, mix1.rearrange("k c d -> k (c d)"),
                IndirectOffsetOnAxis(kinds[:, 1:2].bitcast(u32), 0)).then_inc(rows1_gathered, 16)
            nc.gpsimd.memset(blocks1[:, :], 0.0).then_inc(blocks1_zero, 1)
            pool.wait_ge(rows1_gathered, 16)
            pool.dma_start(gathered1, rows1[:, :]).then_inc(rows1_stored, 16)
            pool.wait_ge(rows1_stored, 16)
            pool.wait_ge(blocks1_zero, 1)
            for s in range(PER_TILE):
                pool.dma_start(
                    blocks1[s * C:(s + 1) * C, :].rearrange("c (n d) -> c n d", d=P)[:, :, s * C:(s + 1) * C],
                    gathered1.rearrange("(n s) (c d) -> s c n d", s=PER_TILE, c=C)[s]).then_inc(blocks1_loaded, 16)

            pool.wait_ge(bias_loaded, 16)

            def add_bias(tile, slot, turn):
                pool.wait_ge(x_loaded[slot], 16 * turn + 16)
                nc.gpsimd.tensor_tensor(out=x1[:, slot, :], in0=x_in[:, slot, :], in1=bias[:, :],
                                        op=ALU.add).then_inc(biased, 1)

            for slot in range(RING):
                add_bias(slot, slot, 0)
            with pool.Fori(1, TILES // RING) as turn:
                for slot in range(RING):
                    pool.wait_ge(stored[slot], 16 * turn)
                    add_bias(None, slot, turn)
            for slot in range(TILES % RING):
                pool.wait_ge(stored[slot], 16 * (TILES // RING))
                add_bias(None, slot, TILES // RING)

        @block.scalar
        def _(act):
            act.dma_start(kinds[:, 0:1], kind0.rearrange("(n a) -> n a", a=1)).then_inc(kinds_loaded, 16)
            act.dma_start(kinds[:, 1:2], kind1.rearrange("(n a) -> n a", a=1)).then_inc(kinds_loaded, 16)
            for to, of in ((c0_sb, coefs0), (c1_sb, coefs1), (m0_sb, mask0), (m1_sb, mask1)):
                act.dma_start(to[:, :, :], of.rearrange("e (p q) r -> p e (q r)", q=CHUNKS)).then_inc(coefs_loaded, 16)
            act.wait_ge(rows0_gathered, 16)
            act.dma_start(gathered0, rows0[:, :]).then_inc(rows0_stored, 16)
            act.wait_ge(rows0_stored, 16)
            act.wait_ge(blocks0_zero, 1)
            for s in range(PER_TILE):
                act.dma_start(
                    blocks0[s * C:(s + 1) * C, :].rearrange("c (n d) -> c n d", d=P)[:, :, s * C:(s + 1) * C],
                    gathered0.rearrange("(n s) (c d) -> s c n d", s=PER_TILE, c=C)[s]).then_inc(blocks0_loaded, 16)

            act.wait_ge(spectrum_done, 1)
            nc.scalar.activation(spectrum[:, :], spectrum_ps, ACT.Copy, scale=SCALING).then_inc(spectrum_ready, 1)
            for k in range(CHUNKS):
                act.wait_ge(a_done, k + 1)
                nc.scalar.activation(a_high[:, k, :], a_ps[k][:, :], ACT.Copy).then_inc(a_high_ready, 1)

            def high0(count):
                act.wait_ge(mixed0, count)
                nc.scalar.activation(y0_high[:, :], y0_ps[:, :], ACT.Copy).then_inc(y0_high_ready, 1)

            def high1(count):
                act.wait_ge(mixed1, count)
                nc.scalar.activation(y1_high[:, :], y1_ps[:, :], ACT.Copy).then_inc(y1_high_ready, 1)

            high0(1)
            high0(2)
            with act.Fori(1, 1 + MIDDLE) as step:
                high1(step)
                high0(step + 2)
            high1(TILES - 1)
            high1(TILES)

        @block.vector
        def _(dve):
            nc.vector.memset(blocks0[:, :], 0.0).then_inc(blocks0_zero, 1)
            dve.wait_ge(coefs_loaded, 64)
            nc.vector.tensor_tensor(out=masked0[:, :, :], in0=c0_sb[:, :, :], in1=m0_sb[:, :, :], op=ALU.mult).then_inc(masked_ready, 1)
            nc.vector.tensor_tensor(out=masked1[:, :, :], in0=c1_sb[:, :, :], in1=m1_sb[:, :, :], op=ALU.mult).then_inc(masked_ready, 1)
            dve.wait_ge(masked_ready, 2)
            nc.vector.tensor_tensor(out=pair0[:, :], in0=masked0[:, 0, :], in1=masked0[:, 1, :], op=ALU.add).then_inc(pairs_ready, 1)
            nc.vector.tensor_tensor(out=pair1[:, :], in0=masked1[:, 0, :], in1=masked1[:, 1, :], op=ALU.add).then_inc(pairs_ready, 1)
            dve.wait_ge(pairs_ready, 2)
            nc.vector.tensor_tensor(out=decode[:, :, 0:R0], in0=pair0[:, :].rearrange("p (q r) -> p q r", r=R0),
                                    in1=masked0[:, 2, :].rearrange("p (q r) -> p q r", r=R0), op=ALU.add).then_inc(decode_ready, 1)
            nc.vector.tensor_tensor(out=decode[:, :, R0:R], in0=pair1[:, :].rearrange("p (q r) -> p q r", r=R1),
                                    in1=masked1[:, 2, :].rearrange("p (q r) -> p q r", r=R1), op=ALU.add).then_inc(decode_ready, 1)
            for k in range(CHUNKS):
                dve.wait_ge(a_high_ready, k + 1)
                nc.vector.tensor_tensor(out=a_low[:, k, :], in0=a_ps[k][:, :], in1=a_high[:, k, :].bitcast(f32),
                                        op=ALU.subtract).then_inc(a_low_ready, 1)

            def low0(count):
                dve.wait_ge(y0_high_ready, count)
                nc.vector.tensor_tensor(out=y0_low[:, :], in0=y0_ps[:, :], in1=y0_high[:, :].bitcast(f32),
                                        op=ALU.subtract).then_inc(y0_low_ready, 1)

            def low1(count):
                dve.wait_ge(y1_high_ready, count)
                nc.vector.tensor_tensor(out=y1_low[:, :], in0=y1_ps[:, :], in1=y1_high[:, :].bitcast(f32),
                                        op=ALU.subtract).then_inc(y1_low_ready, 1)

            def residual0(slot, count):
                dve.wait_ge(biased, count)
                dve.wait_ge(fed0, count)
                nc.vector.tensor_tensor(out=x1[:, slot, :], in0=f0_ps[:, :], in1=x1[:, slot, :],
                                        op=ALU.add).then_inc(x1_ready, 1)

            def residual1(slot, count):
                dve.wait_ge(fed1, count)
                nc.vector.scalar_tensor_tensor(out=x1[:, slot, :], in0=f1_ps[:, :], scalar=scale_sb[:, 0:1],
                                               in1=x1[:, slot, :], op0=ALU.mult, op1=ALU.add).then_inc(out_ready, 1)

            low0(1)
            dve.wait_ge(bits_loaded, 16)
            nc.vector.tensor_scalar(b_sign[:, :, :], bits_sb[:, :, :], 2.0, -1.0, ALU.mult, ALU.add).then_inc(b_ready, 1)
            residual0(0, 1)
            low0(2)
            dve.wait_ge(scale_loaded, 16)
            with dve.Fori(1, 1 + MIDDLE, RING) as base:
                for u in range(RING):
                    low1(base + u)
                    residual0((1 + u) % RING, base + u + 1)
                    low0(base + u + 2)
                    residual1(u, base + u)
            low1(TILES - 1)
            residual0((TILES - 1) % RING, TILES)
            residual1((TILES - 2) % RING, TILES - 1)
            low1(TILES)
            residual1((TILES - 1) % RING, TILES)

        @block.tensor
        def _(pe):
            pe.wait_ge(ident_ready, 1)
            pe.wait_ge(w_loaded, 16)
            for k in range(CHUNKS):
                for c in range(CHUNKS):
                    nc.tensor.matmul(a_ps[k][:, c * P:(c + 1) * P], w_sb[:, c, k * P:(k + 1) * P], ident[:, :],
                                     start=(c == 0), stop=False, is_transpose=True, skip_group_check=True)
            pe.wait_ge(decode_ready, 2)
            pe.wait_ge(basis_loaded, 16)
            for q in range(CHUNKS):
                last = nc.tensor.matmul(spectrum_ps, decode[:, q, :], basis_sb[:, q, :], start=(q == 0), stop=(q == CHUNKS - 1))
            last.then_inc(spectrum_done, 1)

            def mix(to, of, blocks, tile):
                for k in range(CHUNKS):
                    last = nc.tensor.matmul(to[:, k * P:(k + 1) * P], of[:, k * P:(k + 1) * P],
                                            blocks[:, bass.ds(tile * P, P)], start=True, stop=True)
                return last

            pe.wait_ge(blocks0_loaded, 16 * PER_TILE)

            def mix0_tile(tile, slot, turn):
                pe.wait_ge(x_loaded[slot], 16 * turn + 16)
                mix(y0_ps, x_in[:, slot, :], blocks0, tile).then_inc(mixed0, 1)

            def mix1_tile(tile, slot):
                pe.wait_ge(x1_ready, tile + 1)
                mix(y1_ps, x1[:, slot, :], blocks1, tile).then_inc(mixed1, 1)

            def feed0(count):
                pe.wait_ge(y0_high_ready, count)
                for k in range(CHUNKS):
                    for a in (a_high, a_low):
                        nc.tensor.matmul(f0_ps[:, :], y0_high[:, k * P:(k + 1) * P], a[:, k, :],
                                         start=(k == 0 and a is a_high), stop=False)
                pe.wait_ge(y0_low_ready, count)
                for k in range(CHUNKS):
                    last = nc.tensor.matmul(f0_ps[:, :], y0_low[:, k * P:(k + 1) * P], a_high[:, k, :],
                                            start=False, stop=(k == CHUNKS - 1))
                last.then_inc(fed0, 1)

            def feed1(count, first=False):
                if not first:
                    pe.wait_ge(out_ready, count - 1)
                pe.wait_ge(y1_high_ready, count)
                for k in range(CHUNKS):
                    nc.tensor.matmul(f1_ps[:, :], y1_high[:, k * P:(k + 1) * P], b_sign[:, k, :],
                                     start=(k == 0), stop=False)
                pe.wait_ge(y1_low_ready, count)
                for k in range(CHUNKS):
                    last = nc.tensor.matmul(f1_ps[:, :], y1_low[:, k * P:(k + 1) * P], b_sign[:, k, :],
                                            start=False, stop=(k == CHUNKS - 1))
                last.then_inc(fed1, 1)

            mix0_tile(0, 0, 0)
            pe.wait_ge(enc_loaded, 32)
            pe.wait_ge(spectrum_ready, 1)
            for k in range(CHUNKS):
                nc.tensor.matmul(a_ps[k][:, :], enc_sb[:, k * P:(k + 1) * P], spectrum[:, :],
                                 start=False, stop=True, skip_group_check=True).then_inc(a_done, 1)

            pe.wait_ge(a_low_ready, CHUNKS)
            feed0(1)
            mix0_tile(1, 1, 0)
            pe.wait_ge(blocks1_loaded, 16 * PER_TILE)
            pe.wait_ge(b_ready, 1)

            def step(tile, u, turn, first=False):
                mix1_tile(tile - 1, u % RING)
                feed0(tile + 1)
                mix0_tile(tile + 1, (u + 2) % RING, turn)
                feed1(tile, first)

            for u in range(RING):
                step(1 + u, u, (2 + u) // RING, first=(u == 0))
            with pe.Fori(1, MIDDLE // RING) as turn:
                for u in range(RING):
                    step(turn * RING + 1 + u, u, turn + (2 + u) // RING)
            mix1_tile(TILES - 2, (TILES - 2) % RING)
            feed0(TILES)
            feed1(TILES - 1)
            mix1_tile(TILES - 1, (TILES - 1) % RING)
            feed1(TILES)


INPUTS = ["x", "itok_B_0_15", "itok_B_0_30", "L0_cond_weights", "L0_ffn_W_base", "L0_ffn_b_base", "L0_ffn_enc0",
          "L0_ffn_enc1", "L0_ffn_coefs0", "L0_ffn_coefs1", "L0_ffn_mask0", "L0_ffn_mask1", "L1_cond_weights",
          "L1_ffn_kernel", "L1_ffn_scale"]


def kernel(**inputs):
    import concourse.bacc as bacc
    from concourse.bass_utils import run_bass_kernel_spmd

    nc = bacc.Bacc("TRN2", target_bir_lowering=False, num_devices=1)
    arrays = {name: np.ascontiguousarray(inputs[name]) for name in INPUTS}
    arrays["fourier_basis"] = fourier_basis()
    args = [nc.dram_tensor(f"in_{name}", a.shape, mybir.dt.from_np(a.dtype), kind="ExternalInput").ap()
            for name, a in arrays.items()]
    out = nc.dram_tensor("out_x", (SAMPLES, C, T), mybir.dt.float32, kind="ExternalOutput").ap()
    build(nc, *args, out)
    result = run_bass_kernel_spmd(nc, [{f"in_{name}": a for name, a in arrays.items()}], core_ids=[0])
    return result.results[0]["out_x"]
```

```python
from contextlib import ExitStack

import numpy as np
import concourse.bass as bass
from concourse import mybir
from concourse.bass import IndirectOffsetOnAxis

P = 128
SAMPLES, C, T = 128, 32, 512
PER_TILE = P // C
TILES = SAMPLES // PER_TILE
CHUNKS = T // P
KINDS0, KINDS1 = 16, 32
EXPERTS, R0, R1 = 3, 32, 8
R = R0 + R1
SCALING = 16.0 / 32.0
LAYERS = 2
RING = 3
WARM_UP = 12
MIDDLE = TILES - 2


def fourier_basis():
    t = np.arange(T, dtype=np.float64)
    f = np.empty((T, T), np.float64)
    f[0] = 1.0 / np.sqrt(T)
    for k in range(1, (T - 1) // 2 + 1):
        angle = 2.0 * np.pi * ((k * t) % T) / T
        f[2 * k - 1] = np.sqrt(2.0 / T) * np.cos(angle)
        f[2 * k] = np.sqrt(2.0 / T) * np.sin(angle)
    f[T - 1] = np.where(t % 2 == 0, 1.0, -1.0) / np.sqrt(T)
    return f.astype(np.float32)


def build(nc, x, kind0, kind1, mix0, w_base, b_base, enc0, enc1, coefs0, coefs1, mask0, mask1,
          mix1, sign_bits, scale, basis, out):
    f32, f32r, u8 = mybir.dt.float32, mybir.dt.float32r, mybir.dt.uint8
    i32, u32 = mybir.dt.int32, mybir.dt.uint32
    ALU, ACT = mybir.AluOpType, mybir.ActivationFunctionType

    bf16 = mybir.dt.bfloat16
    x_tiles = x.rearrange("(n s) c t -> n (s c) t", s=PER_TILE)
    out_tiles = out.rearrange("(n s) c t -> n (s c) t", s=PER_TILE)
    mix_rows = [mix.rearrange("k c d -> (k c) d") for mix in (mix0, mix1)]

    ctx = ExitStack()
    with ctx:
        def sb(name, shape, dt):
            return ctx.enter_context(nc.sbuf_tensor(name, shape, dt))

        def bank(name):
            return ctx.enter_context(nc.psum_tensor(name, [P, T], f32))

        def sem(name):
            return ctx.enter_context(nc.semaphore(name))

        kinds = sb("kinds", [P, LAYERS, SAMPLES], i32)
        channel = sb("channel", [P, 1], i32)
        partition = sb("partition", [P, 1], i32)
        row_of = sb("row_of", [P, TILES, LAYERS], i32)
        row_now = sb("row_now", [P, RING, LAYERS], i32)
        gathered = sb("gathered", [P, RING, LAYERS, C], f32)
        blocks = sb("blocks", [P, RING, LAYERS, P], f32)
        idle = sb("idle", [P, T], bf16)
        w_sb = sb("w_sb", [P, CHUNKS, T], f32)
        basis_sb = sb("basis_sb", [P, CHUNKS, T], f32)
        c0_sb = sb("c0_sb", [P, EXPERTS, CHUNKS * R0], f32)
        c1_sb = sb("c1_sb", [P, EXPERTS, CHUNKS * R1], f32)
        m0_sb = sb("m0_sb", [P, EXPERTS, CHUNKS * R0], u8)
        m1_sb = sb("m1_sb", [P, EXPERTS, CHUNKS * R1], u8)
        masked0 = sb("masked0", [P, EXPERTS, CHUNKS * R0], f32)
        masked1 = sb("masked1", [P, EXPERTS, CHUNKS * R1], f32)
        pair0 = sb("pair0", [P, CHUNKS * R0], f32)
        pair1 = sb("pair1", [P, CHUNKS * R1], f32)
        decode = sb("decode", [P, CHUNKS, R], f32)
        enc_sb = sb("enc_sb", [R, T], f32)
        spectrum = sb("spectrum", [R, T], f32)
        bits_sb = sb("bits_sb", [P, CHUNKS, T], u8)
        a_high = sb("a_high", [P, CHUNKS, T], f32r)
        a_low = sb("a_low", [P, CHUNKS, T], f32r)
        b_sign = sb("b_sign", [P, CHUNKS, T], f32r)
        ident = sb("ident", [P, P], f32)
        bias = sb("bias", [P, T], f32)
        scale_sb = sb("scale_sb", [P, 1], f32)
        warm = sb("warm", [P, 1], f32)

        x_in = sb("x_in", [P, RING, T], f32)
        x1 = sb("x1", [P, RING, T], f32)
        y0_high = sb("y0_high", [P, T], f32r)
        y0_low = sb("y0_low", [P, T], f32r)
        y1_high = sb("y1_high", [P, T], f32r)
        y1_low = sb("y1_low", [P, T], f32r)

        y0_ps, y1_ps, f0_ps, f1_ps = bank("y0_ps"), bank("y1_ps"), bank("f0_ps"), bank("f1_ps")
        a_ps = [bank(f"a_ps{k}") for k in range(CHUNKS)]
        spectrum_ps = f1_ps[0:R, :]

        kinds_loaded, partition_ready, channel_ready, row_of_ready = sem("partition_ready"), sem("kinds_loaded"), sem("channel_ready"), sem("row_of_ready")
        blocks_zero, idle_zero = sem("blocks_zero"), sem("idle_zero")
        w_loaded = [sem(f"w_loaded{k}") for k in range(CHUNKS)]
        basis_loaded, coefs_loaded = sem("basis_loaded"), sem("coefs_loaded")
        enc_loaded, bits_loaded, bias_loaded, scale_loaded = (
            sem("enc_loaded"), sem("bits_loaded"), sem("bias_loaded"), sem("scale_loaded"))
        ident_zero, ident_ready = sem("ident_zero"), sem("ident_ready")
        masked_ready, pairs_ready, decode_ready = sem("masked_ready"), sem("pairs_ready"), sem("decode_ready")
        spectrum_done, spectrum_ready = sem("spectrum_done"), sem("spectrum_ready")
        a_done, a_high_ready, a_low_ready, b_ready = sem("a_done"), sem("a_high_ready"), sem("a_low_ready"), sem("b_ready")
        x_loaded = [sem(f"x_loaded{s}") for s in range(RING)]
        stored = [sem(f"stored{s}") for s in range(RING)]
        rows_gathered = [sem(f"rows_gathered{s}") for s in range(RING)]
        rows_named = sem("rows_named")
        expanded = sem("expanded")
        biased = sem("biased")
        mixed0, y0_high_ready, y0_low_ready, fed0, x1_ready = (
            sem("mixed0"), sem("y0_high_ready"), sem("y0_low_ready"), sem("fed0"), sem("x1_ready"))
        mixed1, y1_high_ready, y1_low_ready, fed1, out_ready = (
            sem("mixed1"), sem("y1_high_ready"), sem("y1_low_ready"), sem("fed1"), sem("out_ready"))

        block = ctx.enter_context(nc.Block())

        @block.sync
        def _(sp):
            for to, of in ((c0_sb, coefs0), (m0_sb, mask0), (c1_sb, coefs1), (m1_sb, mask1)):
                sp.dma_start(to[:, :, :], of.rearrange("e (p q) r -> p e (q r)", q=CHUNKS)).then_inc(coefs_loaded, 16)
            sp.dma_start(enc_sb[0:R0, :], enc0).then_inc(enc_loaded, 16)
            sp.dma_start(enc_sb[R0:R, :], enc1).then_inc(enc_loaded, 16)
            for k in range(CHUNKS):
                sp.dma_start(w_sb[:, :, k * P:(k + 1) * P], w_base.rearrange("(c p) d -> p c d", p=P)[:, :, k * P:(k + 1) * P]
                             ).then_inc(w_loaded[k], 16)
            sp.dma_start(bias[:, :], b_base.partition_broadcast(P)).then_inc(bias_loaded, 16)
            sp.dma_start(x_in[:, 1, :], x_tiles[1]).then_inc(x_loaded[1], 16)
            sp.dma_start(bits_sb[:, :, :], sign_bits.rearrange("(c p) f -> p c f", p=P)).then_inc(bits_loaded, 16)
            sp.dma_start(scale_sb[:, :], scale.partition_broadcast(P)).then_inc(scale_loaded, 16)
            sp.dma_start(x_in[:, 2, :], x_tiles[2]).then_inc(x_loaded[2], 16)

            def load(tile, slot):
                sp.wait_ge(mixed0, tile - RING + 1)
                sp.wait_ge(biased, tile - RING + 1)
                sp.dma_start(x_in[:, slot, :], x_tiles[bass.ds(tile, 1)].rearrange("a p t -> (a p) t")
                             ).then_inc(x_loaded[slot], 16)

            def store(tile, slot):
                sp.wait_ge(out_ready, tile + 1)
                sp.dma_start(out_tiles[bass.ds(tile, 1)].rearrange("a p t -> (a p) t"), x1[:, slot, :]
                             ).then_inc(stored[slot], 16)

            looped = (TILES - RING) // RING * RING
            with sp.Fori(0, looped, RING) as base:
                for u in range(RING):
                    load(base + u + RING, u)
                    store(base + u, u)
            for tile in range(looped, TILES):
                if tile + RING < TILES:
                    load(tile + RING, tile % RING)
                store(tile, tile % RING)
            for slot in range(RING):
                sp.wait_ge(stored[slot], 16 * len(range(slot, TILES, RING)))

        @block.gpsimd
        def _(pool):
            nc.gpsimd.iota(partition[:, :], pattern=[[0, 1]], base=0, channel_multiplier=1).then_inc(partition_ready, 1)
            nc.gpsimd.memset(ident[:, :], 0.0).then_inc(ident_zero, 1)

            def gather(rows, slot):
                for layer in range(LAYERS):
                    nc.gpsimd.indirect_dma_start(gathered[:, slot, layer, :], None, mix_rows[layer],
                                                 IndirectOffsetOnAxis(rows[:, layer:layer + 1].bitcast(u32), 0)
                                                 ).then_inc(rows_gathered[slot], 16)

            def add_bias(slot, turn):
                pool.wait_ge(x_loaded[slot], 16 * turn + 16)
                nc.gpsimd.tensor_tensor(out=x1[:, slot, :], in0=x_in[:, slot, :], in1=bias[:, :],
                                        op=ALU.add).then_inc(biased, 1)

            def name_rows(tile, slot):
                nc.gpsimd.tensor_copy(row_now[:, slot, :], row_of[:, bass.ds(tile, 1), :].rearrange("p a l -> p (a l)")
                                      ).then_inc(rows_named, 1)

            def prepare(tile, slot, turn, recycled=True, more=True):
                if more:
                    pool.wait_ge(expanded, PER_TILE * (tile + 1))
                    name_rows(tile + RING, slot)
                    pool.wait_ge(rows_named, tile + 1)
                if recycled:
                    pool.wait_ge(stored[slot], 16 * turn)
                add_bias(slot, turn)
                if more:
                    gather(row_now[:, slot, :], slot)

            pool.wait_ge(row_of_ready, PER_TILE)
            gather(row_of[:, 0, :], 0)
            pool.wait_ge(ident_zero, 1)
            nc.gpsimd.affine_select(out=ident[:, :], in_=ident[:, :], compare_op=ALU.not_equal, fill=1.0, base=0,
                                    pattern=[[-1, P]], channel_multiplier=1).then_inc(ident_ready, 1)
            for slot in range(1, RING):
                gather(row_of[:, slot, :], slot)
            pool.wait_ge(bias_loaded, 16)
            for slot in range(RING):
                prepare(slot, slot, 0, recycled=False)
            with pool.Fori(1, TILES // RING - 1) as turn:
                for slot in range(RING):
                    prepare(turn * RING + slot, slot, turn)
            for tile in range((TILES // RING - 1) * RING, TILES):
                prepare(tile, tile % RING, tile // RING, more=(tile + RING < TILES))

        @block.scalar
        def _(act):
            act.dma_start(kinds[:, 0, :], kind0.partition_broadcast(P)).then_inc(kinds_loaded, 16)
            act.dma_start(kinds[:, 1, :], kind1.partition_broadcast(P)).then_inc(kinds_loaded, 16)
            act.dma_start(basis_sb[:, :, :], basis.rearrange("(p q) t -> p q t", q=CHUNKS)).then_inc(basis_loaded, 16)
            act.dma_start(x_in[:, 0, :], x_tiles[0]).then_inc(x_loaded[0], 16)
            act.wait_ge(idle_zero, 1)
            nc.scalar.activation(warm[:, :], idle[:, 0:1], ACT.Copy)

            def expand(slot, turn):
                act.wait_ge(rows_gathered[slot], 16 * LAYERS * (turn + 1))
                for j in range(PER_TILE):
                    part = slice(j * C, (j + 1) * C)
                    nc.scalar.activation(blocks[part, slot, :, part], gathered[part, slot, :, :], ACT.Copy).then_inc(expanded, 1)

            act.wait_ge(blocks_zero, 1)
            expand(0, 0)
            act.wait_ge(spectrum_done, 1)
            nc.scalar.activation(spectrum[:, :], spectrum_ps, ACT.Copy, scale=SCALING).then_inc(spectrum_ready, 1)
            def high0(count):
                act.wait_ge(mixed0, count)
                nc.scalar.activation(y0_high[:, :], y0_ps[:, :], ACT.Copy).then_inc(y0_high_ready, 1)

            def high1(count):
                act.wait_ge(mixed1, count)
                nc.scalar.activation(y1_high[:, :], y1_ps[:, :], ACT.Copy).then_inc(y1_high_ready, 1)

            high0(1)
            for k in range(CHUNKS):
                act.wait_ge(a_done, k + 1)
                nc.scalar.activation(a_high[:, k, :], a_ps[k][:, :], ACT.Copy).then_inc(a_high_ready, 1)
            expand(1, 0)
            expand(2, 0)
            high0(2)
            with act.Fori(0, MIDDLE // RING - 1) as turn:
                for u in range(RING):
                    high1(turn * RING + u + 1)
                    expand(u, turn + 1)
                    high0(turn * RING + u + 3)
            for tile in range(MIDDLE - RING, MIDDLE):
                high1(tile + 1)
                if tile + RING < TILES:
                    expand(tile % RING, tile // RING + 1)
                high0(tile + 3)
            high1(TILES - 1)
            high1(TILES)

        @block.vector
        def _(dve):
            nc.vector.memset(idle[:, :], 0.0).then_inc(idle_zero, 1)
            nc.vector.memset(blocks[:, :, :, :], 0.0).then_inc(blocks_zero, 1)
            dve.wait_ge(partition_ready, 1)
            nc.vector.tensor_scalar(channel[:, :], partition[:, :], C - 1, None, ALU.bitwise_and).then_inc(channel_ready, 1)
            dve.wait_ge(channel_ready, 1)
            dve.wait_ge(kinds_loaded, 16 * LAYERS)
            for j in range(PER_TILE):
                part = slice(j * C, (j + 1) * C)
                nc.vector.tensor_scalar(row_of[part, :, :].rearrange("p n l -> p l n"), kinds[part, :, j::PER_TILE], float(C), channel[part, :],
                                        ALU.mult, ALU.add).then_inc(row_of_ready, 1)
            dve.wait_ge(coefs_loaded, 64)
            nc.vector.tensor_tensor(out=masked0[:, :, :], in0=c0_sb[:, :, :], in1=m0_sb[:, :, :], op=ALU.mult).then_inc(masked_ready, 1)
            nc.vector.tensor_tensor(out=masked1[:, :, :], in0=c1_sb[:, :, :], in1=m1_sb[:, :, :], op=ALU.mult).then_inc(masked_ready, 1)
            dve.wait_ge(masked_ready, 2)
            nc.vector.tensor_tensor(out=pair0[:, :], in0=masked0[:, 0, :], in1=masked0[:, 1, :], op=ALU.add).then_inc(pairs_ready, 1)
            nc.vector.tensor_tensor(out=pair1[:, :], in0=masked1[:, 0, :], in1=masked1[:, 1, :], op=ALU.add).then_inc(pairs_ready, 1)
            dve.wait_ge(pairs_ready, 2)
            nc.vector.tensor_tensor(out=decode[:, :, 0:R0], in0=pair0[:, :].rearrange("p (q r) -> p q r", r=R0),
                                    in1=masked0[:, 2, :].rearrange("p (q r) -> p q r", r=R0), op=ALU.add).then_inc(decode_ready, 1)
            nc.vector.tensor_tensor(out=decode[:, :, R0:R], in0=pair1[:, :].rearrange("p (q r) -> p q r", r=R1),
                                    in1=masked1[:, 2, :].rearrange("p (q r) -> p q r", r=R1), op=ALU.add).then_inc(decode_ready, 1)
            dve.wait_ge(y0_high_ready, 1)
            nc.vector.tensor_tensor(out=y0_low[:, :], in0=y0_ps[:, :], in1=y0_high[:, :].bitcast(f32),
                                    op=ALU.subtract).then_inc(y0_low_ready, 1)
            for k in range(CHUNKS):
                dve.wait_ge(a_high_ready, k + 1)
                nc.vector.tensor_tensor(out=a_low[:, k, :], in0=a_ps[k][:, :], in1=a_high[:, k, :].bitcast(f32),
                                        op=ALU.subtract).then_inc(a_low_ready, 1)

            def low0(count):
                dve.wait_ge(y0_high_ready, count)
                nc.vector.tensor_tensor(out=y0_low[:, :], in0=y0_ps[:, :], in1=y0_high[:, :].bitcast(f32),
                                        op=ALU.subtract).then_inc(y0_low_ready, 1)

            def low1(count):
                dve.wait_ge(y1_high_ready, count)
                nc.vector.tensor_tensor(out=y1_low[:, :], in0=y1_ps[:, :], in1=y1_high[:, :].bitcast(f32),
                                        op=ALU.subtract).then_inc(y1_low_ready, 1)

            def residual0(slot, count):
                dve.wait_ge(biased, count)
                dve.wait_ge(fed0, count)
                nc.vector.tensor_tensor(out=x1[:, slot, :], in0=f0_ps[:, :], in1=x1[:, slot, :],
                                        op=ALU.add).then_inc(x1_ready, 1)

            def residual1(slot, count):
                dve.wait_ge(fed1, count)
                nc.vector.scalar_tensor_tensor(out=x1[:, slot, :], in0=f1_ps[:, :], scalar=scale_sb[:, 0:1],
                                               in1=x1[:, slot, :], op0=ALU.mult, op1=ALU.add).then_inc(out_ready, 1)

            dve.wait_ge(bits_loaded, 16)
            nc.vector.tensor_scalar(b_sign[:, :, :], bits_sb[:, :, :], 2.0, -1.0, ALU.mult, ALU.add).then_inc(b_ready, 1)
            residual0(0, 1)
            low0(2)
            dve.wait_ge(scale_loaded, 16)
            with dve.Fori(1, 1 + MIDDLE, RING) as base:
                for u in range(RING):
                    low1(base + u)
                    residual0((1 + u) % RING, base + u + 1)
                    low0(base + u + 2)
                    residual1(u, base + u)
            low1(TILES - 1)
            residual0((TILES - 1) % RING, TILES)
            residual1((TILES - 2) % RING, TILES - 1)
            low1(TILES)
            residual1((TILES - 1) % RING, TILES)

        @block.tensor
        def _(pe):
            pe.wait_ge(idle_zero, 1)
            for _ in range(WARM_UP):
                nc.tensor.matmul(f0_ps[:, :], idle[:, 0:P], idle[:, :], start=True, stop=True)
            pe.wait_ge(decode_ready, 2)
            pe.wait_ge(basis_loaded, 16)
            for q in range(CHUNKS):
                last = nc.tensor.matmul(spectrum_ps, decode[:, q, :], basis_sb[:, q, :], start=(q == 0), stop=(q == CHUNKS - 1))
            last.then_inc(spectrum_done, 1)

            def mix(to, of, slot, layer):
                for k in range(CHUNKS):
                    last = nc.tensor.matmul(to[:, k * P:(k + 1) * P], of[:, k * P:(k + 1) * P],
                                            blocks[:, slot, layer, :], start=True, stop=True)
                return last

            def mix0_tile(tile, slot, turn):
                pe.wait_ge(x_loaded[slot], 16 * turn + 16)
                pe.wait_ge(expanded, PER_TILE * (tile + 1))
                mix(y0_ps, x_in[:, slot, :], slot, 0).then_inc(mixed0, 1)

            def mix1_tile(tile, slot):
                pe.wait_ge(x1_ready, tile + 1)
                mix(y1_ps, x1[:, slot, :], slot, 1).then_inc(mixed1, 1)

            def feed0(count):
                pe.wait_ge(y0_high_ready, count)
                for k in range(CHUNKS):
                    if type(count) is int and count == 1:
                        pe.wait_ge(a_low_ready, k + 1)
                    for a in (a_high, a_low):
                        nc.tensor.matmul(f0_ps[:, :], y0_high[:, k * P:(k + 1) * P], a[:, k, :],
                                         start=(k == 0 and a is a_high), stop=False)
                pe.wait_ge(y0_low_ready, count)
                for k in range(CHUNKS):
                    last = nc.tensor.matmul(f0_ps[:, :], y0_low[:, k * P:(k + 1) * P], a_high[:, k, :],
                                            start=False, stop=(k == CHUNKS - 1))
                last.then_inc(fed0, 1)

            def feed1(count, first=False):
                if not first:
                    pe.wait_ge(out_ready, count - 1)
                pe.wait_ge(y1_high_ready, count)
                for k in range(CHUNKS):
                    nc.tensor.matmul(f1_ps[:, :], y1_high[:, k * P:(k + 1) * P], b_sign[:, k, :],
                                     start=(k == 0), stop=False)
                pe.wait_ge(y1_low_ready, count)
                for k in range(CHUNKS):
                    last = nc.tensor.matmul(f1_ps[:, :], y1_low[:, k * P:(k + 1) * P], b_sign[:, k, :],
                                            start=False, stop=(k == CHUNKS - 1))
                last.then_inc(fed1, 1)

            mix0_tile(0, 0, 0)
            pe.wait_ge(ident_ready, 1)
            pe.wait_ge(enc_loaded, 32)
            for k in range(CHUNKS):
                pe.wait_ge(w_loaded[k], 16)
                for c in range(CHUNKS):
                    nc.tensor.matmul(a_ps[k][:, c * P:(c + 1) * P], w_sb[:, c, k * P:(k + 1) * P], ident[:, :],
                                     start=(c == 0), stop=False, is_transpose=True, skip_group_check=True)
                if k == 0:
                    pe.wait_ge(spectrum_ready, 1)
                nc.tensor.matmul(a_ps[k][:, :], enc_sb[:, k * P:(k + 1) * P], spectrum[:, :],
                                 start=False, stop=True, skip_group_check=True).then_inc(a_done, 1)

            feed0(1)
            mix0_tile(1, 1, 0)
            pe.wait_ge(b_ready, 1)

            def step(tile, u, turn, first=False):
                mix1_tile(tile - 1, u % RING)
                feed0(tile + 1)
                mix0_tile(tile + 1, (u + 2) % RING, turn)
                feed1(tile, first)

            for u in range(RING):
                step(1 + u, u, (2 + u) // RING, first=(u == 0))
            with pe.Fori(1, MIDDLE // RING) as turn:
                for u in range(RING):
                    step(turn * RING + 1 + u, u, turn + (2 + u) // RING)
            mix1_tile(TILES - 2, (TILES - 2) % RING)
            feed0(TILES)
            feed1(TILES - 1)
            mix1_tile(TILES - 1, (TILES - 1) % RING)
            feed1(TILES)


INPUTS = ["x", "itok_B_0_15", "itok_B_0_30", "L0_cond_weights", "L0_ffn_W_base", "L0_ffn_b_base", "L0_ffn_enc0",
          "L0_ffn_enc1", "L0_ffn_coefs0", "L0_ffn_coefs1", "L0_ffn_mask0", "L0_ffn_mask1", "L1_cond_weights",
          "L1_ffn_kernel", "L1_ffn_scale"]


def kernel(**inputs):
    import concourse.bacc as bacc
    from concourse.bass_utils import run_bass_kernel_spmd

    nc = bacc.Bacc("TRN2", target_bir_lowering=False, num_devices=1)
    arrays = {name: np.ascontiguousarray(inputs[name]) for name in INPUTS}
    arrays["fourier_basis"] = fourier_basis()
    args = [nc.dram_tensor(f"in_{name}", a.shape, mybir.dt.from_np(a.dtype), kind="ExternalInput").ap()
            for name, a in arrays.items()]
    out = nc.dram_tensor("out_x", (SAMPLES, C, T), mybir.dt.float32, kind="ExternalOutput").ap()
    build(nc, *args, out)
    result = run_bass_kernel_spmd(nc, [{f"in_{name}": a for name, a in arrays.items()}], core_ids=[0])
    return result.results[0]["out_x"]
```

```python
from contextlib import ExitStack

import numpy as np
import concourse.bass as bass
from concourse import mybir
from concourse.bass import IndirectOffsetOnAxis

P = 128
SAMPLES, C, T = 128, 32, 512
PER_TILE = P // C
TILES = SAMPLES // PER_TILE
CHUNKS = T // P
KINDS0, KINDS1 = 16, 32
EXPERTS, R0, R1 = 3, 32, 8
R = R0 + R1
HALF = T // 2 + 1
SCALING = 16.0 / 32.0
LAYERS = 2
RING = 3
FIRST_MIX = 2
MIDDLE = TILES - 2


def fourier_basis():
    t = np.arange(HALF, dtype=np.float64)
    f = np.empty((T, HALF), np.float64)
    f[0] = 1.0 / np.sqrt(T)
    for k in range(1, (T - 1) // 2 + 1):
        angle = 2.0 * np.pi * ((k * t) % T) / T
        f[2 * k - 1] = np.sqrt(2.0 / T) * np.cos(angle)
        f[2 * k] = np.sqrt(2.0 / T) * np.sin(angle)
        f[2 * k, t * 2 % T == 0] = 0.0
    f[T - 1] = np.where(t % 2 == 0, 1.0, -1.0) / np.sqrt(T)
    return np.ascontiguousarray(f.reshape(P, CHUNKS // 2, 2, HALF).transpose(2, 0, 1, 3).astype(np.float32))


def build(nc, x, kind0, kind1, mix0, w_base, b_base, enc0, enc1, coefs0, coefs1, mask0, mask1,
          mix1, sign_bits, scale, basis, out):
    f32, f32r, u8 = mybir.dt.float32, mybir.dt.float32r, mybir.dt.uint8
    i32, u32 = mybir.dt.int32, mybir.dt.uint32
    ALU, ACT = mybir.AluOpType, mybir.ActivationFunctionType

    bf16 = mybir.dt.bfloat16
    x_tiles = x.rearrange("(n s) c t -> n (s c) t", s=PER_TILE)
    out_tiles = out.rearrange("(n s) c t -> n (s c) t", s=PER_TILE)
    mix_rows = [mix.rearrange("k c d -> (k c) d") for mix in (mix0, mix1)]

    ctx = ExitStack()
    with ctx:
        def sb(name, shape, dt):
            return ctx.enter_context(nc.sbuf_tensor(name, shape, dt))

        def bank(name):
            return ctx.enter_context(nc.psum_tensor(name, [P, T], f32))

        def sem(name):
            return ctx.enter_context(nc.semaphore(name))

        kinds = sb("kinds", [P, LAYERS, SAMPLES], i32)
        channel = sb("channel", [P, 1], i32)
        partition = sb("partition", [P, 1], i32)
        row_of = sb("row_of", [P, TILES, LAYERS], i32)
        row_now = sb("row_now", [P, RING, LAYERS], i32)
        gathered = sb("gathered", [P, RING, LAYERS, C], f32)
        blocks = sb("blocks", [P, RING, LAYERS, P], f32)
        idle = sb("idle", [P, T], bf16)
        w_sb = sb("w_sb", [P, CHUNKS, T], f32)
        basis_sb = sb("basis_sb", [P, 2, CHUNKS // 2, HALF], f32)
        coefs_sb = sb("coefs_sb", [P, EXPERTS, CHUNKS * R], f32)
        masks_sb = sb("masks_sb", [P, EXPERTS, CHUNKS * R], u8)
        masked = sb("masked", [P, EXPERTS, CHUNKS * R], f32)
        pair = sb("pair", [P, CHUNKS * R], f32)
        decode = sb("decode", [P, CHUNKS, P], f32)
        enc_sb = sb("enc_sb", [P, T], f32)
        odd_part = sb("odd_part", [P, HALF], f32)
        mirrored = sb("mirrored", [P, HALF], f32)
        constant2 = sb("constant2", [P, 1], f32)
        spectrum = sb("spectrum", [P, T], f32)
        bits_sb = sb("bits_sb", [P, CHUNKS, T], u8)
        a_high = sb("a_high", [P, CHUNKS, T], f32r)
        a_low = sb("a_low", [P, CHUNKS, T], f32r)
        b_sign = sb("b_sign", [P, CHUNKS, T], f32r)
        ident = sb("ident", [P, P], f32)
        bias = sb("bias", [P, T], f32)
        scale_sb = sb("scale_sb", [P, 1], f32)
        warm = sb("warm", [P, 1], f32)

        x_in = sb("x_in", [P, RING, T], f32)
        x1 = sb("x1", [P, RING, T], f32)
        y0_high = sb("y0_high", [P, T], f32r)
        y0_low = sb("y0_low", [P, T], f32r)
        y1_high = sb("y1_high", [P, T], f32r)
        y1_low = sb("y1_low", [P, T], f32r)

        y0_ps, y1_ps, f0_ps, f1_ps = bank("y0_ps"), bank("y1_ps"), bank("f0_ps"), bank("f1_ps")
        a_ps = [bank(f"a_ps{k}") for k in range(CHUNKS)]
        halves = [slice(half * T // 2, (half + 1) * T // 2) for half in range(2)]
        end_ps = [a_ps[half][:, 0:T // 2] for half in range(2)]
        mirror_sides = [slice(0, HALF), slice(HALF, T)]
        odd_ps, even_ps = y1_ps[:, 0:HALF], f1_ps[:, 0:HALF]

        kinds_loaded, partition_ready, channel_ready, row_of_ready = (
            sem("kinds_loaded"), sem("partition_ready"), sem("channel_ready"), sem("row_of_ready"))
        blocks_zero, idle_zero = sem("blocks_zero"), sem("idle_zero")
        w_loaded = [sem(f"w_loaded{half}") for half in range(2)]
        basis_loaded = [sem(f"basis_loaded{parity}") for parity in range(2)]
        coefs_loaded, masks_loaded = sem("coefs_loaded"), sem("masks_loaded")
        enc_loaded, bits_loaded, bias_loaded, scale_loaded = (
            sem("enc_loaded"), sem("bits_loaded"), sem("bias_loaded"), sem("scale_loaded"))
        ident_zero, ident_ready = sem("ident_zero"), sem("ident_ready")
        masked_ready, pair_ready, decode_ready = sem("masked_ready"), sem("pair_ready"), sem("decode_ready")
        enc_zero, decode_zero = sem("enc_zero"), sem("decode_zero")
        odd_done, even_done, odd_ready = sem("odd_done"), sem("even_done"), sem("odd_ready")
        constant_ready, mirrored_ready, spectrum_ready = sem("constant_ready"), sem("mirrored_ready"), sem("spectrum_ready")
        a_done, a_high_ready, a_low_ready, b_ready = sem("a_done"), sem("a_high_ready"), sem("a_low_ready"), sem("b_ready")
        x_loaded = [sem(f"x_loaded{s}") for s in range(RING)]
        stored = [sem(f"stored{s}") for s in range(RING)]
        rows_gathered = [sem(f"rows_gathered{s}") for s in range(RING)]
        rows_named = sem("rows_named")
        expanded = sem("expanded")
        ended = sem("ended")
        biased = sem("biased")
        mixed0, y0_high_ready, y0_low_ready, fed0, x1_ready = (
            sem("mixed0"), sem("y0_high_ready"), sem("y0_low_ready"), sem("fed0"), sem("x1_ready"))
        mixed1, y1_high_ready, y1_low_ready, fed1, out_ready = (
            sem("mixed1"), sem("y1_high_ready"), sem("y1_low_ready"), sem("fed1"), sem("out_ready"))

        block = ctx.enter_context(nc.Block())

        def load_w(queue, half):
            part = slice(half * T // 2, (half + 1) * T // 2)
            queue.dma_start(w_sb[:, :, part], w_base.rearrange("(c p) d -> p c d", p=P)[:, :, part]).then_inc(w_loaded[half], 16)

        @block.sync
        def _(sp):
            sp.dma_start(kinds[:, 0, :], kind0.partition_broadcast(P)).then_inc(kinds_loaded, 16)
            load_w(sp, 0)
            sp.dma_start(coefs_sb[:, :, CHUNKS * R0:], coefs1.rearrange("e (p q) r -> p e (q r)", q=CHUNKS)).then_inc(coefs_loaded, 16)
            sp.dma_start(basis_sb[:, 1], basis[1]).then_inc(basis_loaded[1], 16)
            sp.wait_ge(enc_zero, 1)
            sp.dma_start(enc_sb[0:R0, :], enc0).then_inc(enc_loaded, 16)
            sp.dma_start(enc_sb[R0:R, :], enc1).then_inc(enc_loaded, 16)
            sp.dma_start(bias[:, :], b_base.partition_broadcast(P)).then_inc(bias_loaded, 16)
            sp.dma_start(x_in[:, 1, :], x_tiles[1]).then_inc(x_loaded[1], 16)
            sp.dma_start(bits_sb[:, :, :], sign_bits.rearrange("(c p) f -> p c f", p=P)).then_inc(bits_loaded, 16)
            sp.dma_start(scale_sb[:, :], scale.partition_broadcast(P)).then_inc(scale_loaded, 16)
            sp.dma_start(x_in[:, 2, :], x_tiles[2]).then_inc(x_loaded[2], 16)

            def load(tile, slot):
                sp.wait_ge(mixed0, tile - RING + 1)
                sp.wait_ge(biased, tile - RING + 1)
                sp.dma_start(x_in[:, slot, :], x_tiles[bass.ds(tile, 1)].rearrange("a p t -> (a p) t")
                             ).then_inc(x_loaded[slot], 16)

            def store(tile, slot):
                sp.wait_ge(out_ready, tile + 1)
                sp.dma_start(out_tiles[bass.ds(tile, 1)].rearrange("a p t -> (a p) t"), x1[:, slot, :]
                             ).then_inc(stored[slot], 16)

            looped = (TILES - RING) // RING * RING
            with sp.Fori(0, looped, RING) as base:
                for u in range(RING):
                    load(base + u + RING, u)
                    store(base + u, u)
            for tile in range(looped, TILES - 1):
                if tile + RING < TILES:
                    load(tile + RING, tile % RING)
                store(tile, tile % RING)
            for half, columns in enumerate(halves):
                sp.wait_ge(out_ready, TILES + half)
                sp.dma_start(out_tiles[TILES - 1][:, columns], x1[:, (TILES - 1) % RING, columns]).then_inc(ended, 16)
            for slot in range(RING):
                sp.wait_ge(stored[slot], 16 * len(range(slot, TILES - 1, RING)))
            sp.wait_ge(ended, 32)

        @block.gpsimd
        def _(pool):
            pool.dma_start(masks_sb[:, :, 0:CHUNKS * R0], mask0.rearrange("e (p q) r -> p e (q r)", q=CHUNKS)).then_inc(masks_loaded, 16)
            pool.dma_start(masks_sb[:, :, CHUNKS * R0:], mask1.rearrange("e (p q) r -> p e (q r)", q=CHUNKS)).then_inc(masks_loaded, 16)
            nc.gpsimd.iota(partition[:, :], pattern=[[0, 1]], base=0, channel_multiplier=1).then_inc(partition_ready, 1)
            nc.gpsimd.memset(ident[:, :], 0.0).then_inc(ident_zero, 1)
            pool.wait_ge(ident_zero, 1)
            nc.gpsimd.affine_select(out=ident[:, :], in_=ident[:, :], compare_op=ALU.not_equal, fill=1.0, base=0,
                                    pattern=[[-1, P]], channel_multiplier=1).then_inc(ident_ready, 1)
            nc.gpsimd.memset(enc_sb[:, :], 0.0).then_inc(enc_zero, 1)

            def gather(rows, slot):
                for layer in range(LAYERS):
                    nc.gpsimd.indirect_dma_start(gathered[:, slot, layer, :], None, mix_rows[layer],
                                                 IndirectOffsetOnAxis(rows[:, layer:layer + 1].bitcast(u32), 0)
                                                 ).then_inc(rows_gathered[slot], 16)

            def add_bias(slot, turn):
                pool.wait_ge(x_loaded[slot], 16 * turn + 16)
                nc.gpsimd.tensor_tensor(out=x1[:, slot, :], in0=x_in[:, slot, :], in1=bias[:, :],
                                        op=ALU.add).then_inc(biased, 1)

            def name_rows(tile, slot):
                nc.gpsimd.tensor_copy(row_now[:, slot, :], row_of[:, bass.ds(tile, 1), :].rearrange("p a l -> p (a l)")
                                      ).then_inc(rows_named, 1)

            def prepare(tile, slot, turn, recycled=True, more=True):
                if more:
                    pool.wait_ge(expanded, PER_TILE * (tile + 1))
                    name_rows(tile + RING, slot)
                    pool.wait_ge(rows_named, tile + 1)
                if recycled:
                    pool.wait_ge(stored[slot], 16 * turn)
                add_bias(slot, turn)
                if more:
                    gather(row_now[:, slot, :], slot)

            pool.wait_ge(row_of_ready, PER_TILE)
            gather(row_of[:, 0, :], 0)
            for slot in range(1, RING):
                gather(row_of[:, slot, :], slot)
            pool.wait_ge(bias_loaded, 16)
            for slot in range(RING):
                prepare(slot, slot, 0, recycled=False)
            with pool.Fori(1, TILES // RING - 1) as turn:
                for slot in range(RING):
                    prepare(turn * RING + slot, slot, turn)
            for tile in range((TILES // RING - 1) * RING, TILES):
                prepare(tile, tile % RING, tile // RING, more=(tile + RING < TILES))

        @block.scalar
        def _(act):
            act.dma_start(kinds[:, 1, :], kind1.partition_broadcast(P)).then_inc(kinds_loaded, 16)
            act.dma_start(coefs_sb[:, :, 0:CHUNKS * R0], coefs0.rearrange("e (p q) r -> p e (q r)", q=CHUNKS)).then_inc(coefs_loaded, 16)
            act.dma_start(basis_sb[:, 0], basis[0]).then_inc(basis_loaded[0], 16)
            load_w(act, 1)
            act.dma_start(x_in[:, 0, :], x_tiles[0]).then_inc(x_loaded[0], 16)
            act.wait_ge(idle_zero, 1)
            nc.scalar.activation(warm[:, :], idle[:, 0:1], ACT.Copy)

            def expand(slot, turn):
                act.wait_ge(rows_gathered[slot], 16 * LAYERS * (turn + 1))
                for j in range(PER_TILE):
                    part = slice(j * C, (j + 1) * C)
                    nc.scalar.activation(blocks[part, slot, :, part], gathered[part, slot, :, :], ACT.Copy).then_inc(expanded, 1)

            act.wait_ge(odd_done, 1)
            nc.scalar.activation(odd_part[:, :], odd_ps, ACT.Copy, scale=SCALING).then_inc(odd_ready, 1)
            act.wait_ge(blocks_zero, 1)
            expand(0, 0)
            def high0(count):
                act.wait_ge(mixed0, count)
                nc.scalar.activation(y0_high[:, :], y0_ps[:, :], ACT.Copy).then_inc(y0_high_ready, 1)

            def high1(count):
                act.wait_ge(mixed1, count)
                nc.scalar.activation(y1_high[:, :], y1_ps[:, :], ACT.Copy).then_inc(y1_high_ready, 1)

            for k in range(CHUNKS):
                if k == FIRST_MIX:
                    high0(1)
                act.wait_ge(a_done, k + 1)
                nc.scalar.activation(a_high[:, k, :], a_ps[k][:, :], ACT.Copy).then_inc(a_high_ready, 1)
            expand(1, 0)
            expand(2, 0)
            high0(2)
            with act.Fori(0, MIDDLE // RING - 1) as turn:
                for u in range(RING):
                    high1(turn * RING + u + 1)
                    expand(u, turn + 1)
                    high0(turn * RING + u + 3)
            for tile in range(MIDDLE - RING, MIDDLE):
                high1(tile + 1)
                if tile + RING < TILES:
                    expand(tile % RING, tile // RING + 1)
                high0(tile + 3)
            high1(TILES - 1)
            high1(TILES)

        @block.vector
        def _(dve):
            nc.vector.memset(idle[:, :], 0.0).then_inc(idle_zero, 1)
            nc.vector.memset(blocks[:, :, :, :], 0.0).then_inc(blocks_zero, 1)
            nc.vector.memset(decode[:, :, :], 0.0).then_inc(decode_zero, 1)
            dve.wait_ge(partition_ready, 1)
            nc.vector.tensor_scalar(channel[:, :], partition[:, :], C - 1, None, ALU.bitwise_and).then_inc(channel_ready, 1)
            dve.wait_ge(channel_ready, 1)
            dve.wait_ge(kinds_loaded, 16 * LAYERS)
            for j in range(PER_TILE):
                part = slice(j * C, (j + 1) * C)
                nc.vector.tensor_scalar(row_of[part, :, :].rearrange("p n l -> p l n"), kinds[part, :, j::PER_TILE], float(C), channel[part, :],
                                        ALU.mult, ALU.add).then_inc(row_of_ready, 1)
            dve.wait_ge(coefs_loaded, 32)
            dve.wait_ge(masks_loaded, 32)
            nc.vector.tensor_tensor(out=masked[:, :, :], in0=coefs_sb[:, :, :], in1=masks_sb[:, :, :], op=ALU.mult).then_inc(masked_ready, 1)
            dve.wait_ge(masked_ready, 1)
            nc.vector.tensor_tensor(out=pair[:, :], in0=masked[:, 0, :], in1=masked[:, 1, :], op=ALU.add).then_inc(pair_ready, 1)
            dve.wait_ge(pair_ready, 1)
            dve.wait_ge(decode_zero, 1)
            for first, rank, at in ((0, R0, 0), (CHUNKS * R0, R1, R0)):
                part = slice(first, first + CHUNKS * rank)
                nc.vector.tensor_tensor(out=decode[:, :, at:at + rank], in0=pair[:, part].rearrange("p (q r) -> p q r", r=rank),
                                        in1=masked[:, 2, part].rearrange("p (q r) -> p q r", r=rank), op=ALU.add).then_inc(decode_ready, 1)
            dve.wait_ge(odd_ready, 1)
            nc.vector.tensor_scalar(constant2[:, :], odd_part[:, 0:1], 2.0, None, ALU.mult).then_inc(constant_ready, 1)
            dve.wait_ge(constant_ready, 1)
            nc.vector.tensor_scalar(mirrored[:, :], odd_part[:, :], -1.0, constant2[:, :], ALU.mult, ALU.add).then_inc(mirrored_ready, 1)
            dve.wait_ge(mirrored_ready, 1)
            dve.wait_ge(even_done, 1)
            nc.vector.scalar_tensor_tensor(out=spectrum[:, 0:HALF], in0=even_ps, scalar=SCALING, in1=odd_part[:, :],
                                           op0=ALU.mult, op1=ALU.add).then_inc(spectrum_ready, 1)
            nc.vector.scalar_tensor_tensor(out=spectrum[:, T - 1:HALF - 1:-1], in0=even_ps[:, 1:HALF - 1], scalar=SCALING,
                                           in1=mirrored[:, 1:HALF - 1], op0=ALU.mult, op1=ALU.add).then_inc(spectrum_ready, 1)
            def low0(count):
                dve.wait_ge(y0_high_ready, count)
                nc.vector.tensor_tensor(out=y0_low[:, :], in0=y0_ps[:, :], in1=y0_high[:, :].bitcast(f32),
                                        op=ALU.subtract).then_inc(y0_low_ready, 1)

            def low1(count):
                dve.wait_ge(y1_high_ready, count)
                nc.vector.tensor_tensor(out=y1_low[:, :], in0=y1_ps[:, :], in1=y1_high[:, :].bitcast(f32),
                                        op=ALU.subtract).then_inc(y1_low_ready, 1)

            def residual0(slot, count):
                dve.wait_ge(biased, count)
                dve.wait_ge(fed0, count)
                nc.vector.tensor_tensor(out=x1[:, slot, :], in0=f0_ps[:, :], in1=x1[:, slot, :],
                                        op=ALU.add).then_inc(x1_ready, 1)

            def residual1(slot, count):
                dve.wait_ge(fed1, count)
                nc.vector.scalar_tensor_tensor(out=x1[:, slot, :], in0=f1_ps[:, :], scalar=scale_sb[:, 0:1],
                                               in1=x1[:, slot, :], op0=ALU.mult, op1=ALU.add).then_inc(out_ready, 1)

            for k in range(CHUNKS):
                if k == FIRST_MIX:
                    low0(1)
                dve.wait_ge(a_high_ready, k + 1)
                nc.vector.tensor_tensor(out=a_low[:, k, :], in0=a_ps[k][:, :], in1=a_high[:, k, :].bitcast(f32),
                                        op=ALU.subtract).then_inc(a_low_ready, 1)
            residual0(0, 1)
            dve.wait_ge(bits_loaded, 16)
            nc.vector.tensor_scalar(b_sign[:, :, :], bits_sb[:, :, :], 2.0, -1.0, ALU.mult, ALU.add).then_inc(b_ready, 1)
            low0(2)
            dve.wait_ge(scale_loaded, 16)
            with dve.Fori(1, 1 + MIDDLE, RING) as base:
                for u in range(RING):
                    low1(base + u)
                    residual0((1 + u) % RING, base + u + 1)
                    low0(base + u + 2)
                    residual1(u, base + u)
            low1(TILES - 1)
            residual0((TILES - 1) % RING, TILES)
            dve.wait_ge(fed1, TILES - 1)
            low1(TILES)
            residual1((TILES - 2) % RING, TILES - 1)
            for half, columns in enumerate(halves):
                dve.wait_ge(fed1, TILES + half)
                nc.vector.scalar_tensor_tensor(out=x1[:, (TILES - 1) % RING, columns], in0=end_ps[half], scalar=scale_sb[:, 0:1],
                                               in1=x1[:, (TILES - 1) % RING, columns], op0=ALU.mult, op1=ALU.add).then_inc(out_ready, 1)

        @block.tensor
        def _(pe):
            pe.wait_ge(idle_zero, 1)
            def warm_up(count):
                for _ in range(count):
                    nc.tensor.matmul(f0_ps[:, :], idle[:, 0:P], idle[:, :], start=True, stop=True)

            def turn_w(half):
                pe.wait_ge(w_loaded[half], 16)
                for k in (2 * half, 2 * half + 1):
                    for c in range(CHUNKS):
                        nc.tensor.matmul(a_ps[k][:, c * P:(c + 1) * P], w_sb[:, c, k * P:(k + 1) * P], ident[:, :],
                                         start=(c == 0), stop=False, is_transpose=True, skip_group_check=True)

            warm_up(10)
            pe.wait_ge(ident_ready, 1)
            turn_w(0)
            warm_up(2)
            pe.wait_ge(decode_ready, 2)
            for parity, to, done in ((0, odd_ps, odd_done), (1, even_ps, even_done)):
                pe.wait_ge(basis_loaded[parity], 16)
                for n in range(CHUNKS // 2):
                    last = nc.tensor.matmul(to, decode[:, 2 * n + parity, :], basis_sb[:, parity, n, :],
                                            start=(n == 0), stop=(n == CHUNKS // 2 - 1))
                last.then_inc(done, 1)

            def mix(to, of, slot, layer):
                for k in range(CHUNKS):
                    last = nc.tensor.matmul(to[:, k * P:(k + 1) * P], of[:, k * P:(k + 1) * P],
                                            blocks[:, slot, layer, :], start=True, stop=True)
                return last

            def mix0_tile(tile, slot, turn):
                pe.wait_ge(x_loaded[slot], 16 * turn + 16)
                pe.wait_ge(expanded, PER_TILE * (tile + 1))
                mix(y0_ps, x_in[:, slot, :], slot, 0).then_inc(mixed0, 1)

            def mix1_tile(tile, slot):
                pe.wait_ge(x1_ready, tile + 1)
                mix(y1_ps, x1[:, slot, :], slot, 1).then_inc(mixed1, 1)

            def feed0(count, first=False):
                pe.wait_ge(y0_high_ready, count)

                def high(k):
                    if first:
                        pe.wait_ge(a_low_ready, k + 1)
                    for a in (a_high, a_low):
                        last = nc.tensor.matmul(f0_ps[:, :], y0_high[:, k * P:(k + 1) * P], a[:, k, :],
                                                start=(k == 0 and a is a_high), stop=(k == CHUNKS - 1 and a is a_low))
                    return last

                for k in range(CHUNKS - 1):
                    high(k)
                pe.wait_ge(y0_low_ready, count)
                if first:
                    pe.wait_ge(a_high_ready, CHUNKS)
                for k in range(CHUNKS):
                    nc.tensor.matmul(f0_ps[:, :], y0_low[:, k * P:(k + 1) * P], a_high[:, k, :], start=False, stop=False)
                high(CHUNKS - 1).then_inc(fed0, 1)

            def feed1_high(count, to=f1_ps[:, :], columns=slice(0, T)):
                pe.wait_ge(y1_high_ready, count)
                for k in range(CHUNKS):
                    nc.tensor.matmul(to, y1_high[:, k * P:(k + 1) * P], b_sign[:, k, columns], start=(k == 0), stop=False)

            def feed1_low(count, to=f1_ps[:, :], columns=slice(0, T)):
                pe.wait_ge(y1_low_ready, count)
                for k in range(CHUNKS):
                    last = nc.tensor.matmul(to, y1_low[:, k * P:(k + 1) * P], b_sign[:, k, columns],
                                            start=False, stop=(k == CHUNKS - 1))
                last.then_inc(fed1, 1)

            turn_w(1)
            pe.wait_ge(enc_loaded, 32)
            for k in range(CHUNKS):
                if k == FIRST_MIX:
                    mix0_tile(0, 0, 0)
                for n, columns in enumerate(mirror_sides if k == 0 else [slice(0, T)]):
                    if k == 0:
                        pe.wait_ge(spectrum_ready, n + 1)
                    last = nc.tensor.matmul(a_ps[k][:, columns], enc_sb[:, k * P:(k + 1) * P], spectrum[:, columns],
                                            start=False, stop=True, skip_group_check=True)
                last.then_inc(a_done, 1)

            feed0(1, first=True)
            mix0_tile(1, 1, 0)

            def step(tile, u, turn, first=False):
                mix1_tile(tile - 1, u % RING)
                feed0(tile + 1)
                mix0_tile(tile + 1, (u + 2) % RING, turn)
                if first:
                    pe.wait_ge(b_ready, 1)
                else:
                    pe.wait_ge(out_ready, tile - 1)
                feed1_high(tile)
                feed1_low(tile)

            for u in range(RING):
                step(1 + u, u, (2 + u) // RING, first=(u == 0))
            with pe.Fori(1, MIDDLE // RING) as turn:
                for u in range(RING):
                    step(turn * RING + 1 + u, u, turn + (2 + u) // RING)
            mix1_tile(TILES - 2, (TILES - 2) % RING)
            feed0(TILES)
            pe.wait_ge(out_ready, TILES - 2)
            feed1_high(TILES - 1)
            mix1_tile(TILES - 1, (TILES - 1) % RING)
            feed1_low(TILES - 1)
            for half in range(2):
                feed1_high(TILES, end_ps[half], halves[half])
            for half in range(2):
                feed1_low(TILES, end_ps[half], halves[half])


INPUTS = ["x", "itok_B_0_15", "itok_B_0_30", "L0_cond_weights", "L0_ffn_W_base", "L0_ffn_b_base", "L0_ffn_enc0",
          "L0_ffn_enc1", "L0_ffn_coefs0", "L0_ffn_coefs1", "L0_ffn_mask0", "L0_ffn_mask1", "L1_cond_weights",
          "L1_ffn_kernel", "L1_ffn_scale"]


def kernel(**inputs):
    import concourse.bacc as bacc
    from concourse.bass_utils import run_bass_kernel_spmd

    nc = bacc.Bacc("TRN2", target_bir_lowering=False, num_devices=1)
    arrays = {name: np.ascontiguousarray(inputs[name]) for name in INPUTS}
    arrays["fourier_basis"] = fourier_basis()
    args = [nc.dram_tensor(f"in_{name}", a.shape, mybir.dt.from_np(a.dtype), kind="ExternalInput").ap()
            for name, a in arrays.items()]
    out = nc.dram_tensor("out_x", (SAMPLES, C, T), mybir.dt.float32, kind="ExternalOutput").ap()
    build(nc, *args, out)
    result = run_bass_kernel_spmd(nc, [{f"in_{name}": a for name, a in arrays.items()}], core_ids=[0])
    return result.results[0]["out_x"]
```
